# Optimizing a Trainium2 kernel written in Bass

```python
import numpy as np
import jax
import jax.numpy as jnp

def _softmax(x, axis=-1):
    return jax.nn.softmax(x, axis=axis)

def _gelu(x):
    return jax.nn.gelu(x, approximate=True)

def _silu(x):
    return jax.nn.silu(x)

def _sigmoid(x):
    return jax.nn.sigmoid(x)

def _layernorm(x, axis=-1, eps=1e-05):
    m = jnp.mean(x, axis=axis, keepdims=True)
    v = jnp.var(x, axis=axis, keepdims=True)
    return (x - m) / jnp.sqrt(v + eps)

def _scatter_add(tgt, idx, src, axis=0):
    return tgt.at[idx].add(src)

def _segment_sum(src, seg, n):
    return jax.ops.segment_sum(src, seg, n)
kernel_name = 'mk_conv_seq_d1_conv_nchw256_r4_f70084'

def setup_inputs(seed: int=0):
    np.random.seed(seed)
    _w = jnp.asarray

    def _rec_inputs():
        import jax
        import jax.numpy as jnp
        _gk = jax.random.key(seed)
        x = -0.0002091 + 1 * jax.random.normal(jax.random.fold_in(_gk, 1), (32, 64, 56, 56), jnp.float32)
        return x
    x = _rec_inputs()

    def _L0_conv_setup():
        import jax, jax.numpy as jnp
        import numpy as np
        EPS = 1e-05

        def _conv3x3(x, w, stride=1):
            return jax.lax.conv_general_dilated(x, w, window_strides=(stride, stride), padding=((1, 1), (1, 1)), dimension_numbers=('NCHW', 'OIHW', 'NCHW'))

        def _bn(x, gamma, beta, mean, var):
            inv = gamma * jax.lax.rsqrt(var + EPS)
            return x * inv[None, :, None, None] + (beta - mean * inv)[None, :, None, None]
        key = jax.random.key(seed)
        ks = jax.random.split(key, 11)
        N, C, H, W = (32, 64, 56, 56)
        x = jax.random.normal(ks[0], (N, C, H, W), dtype=jnp.float32)
        fan = C * 9
        w1 = jax.random.normal(ks[1], (C, C, 3, 3), dtype=jnp.float32) / np.sqrt(fan)
        w2 = jax.random.normal(ks[2], (C, C, 3, 3), dtype=jnp.float32) / np.sqrt(fan)
        g1 = jax.random.uniform(ks[3], (C,), dtype=jnp.float32, minval=0.5, maxval=1.5)
        b1 = jax.random.normal(ks[4], (C,), dtype=jnp.float32) * 0.1
        m1 = jax.random.normal(ks[5], (C,), dtype=jnp.float32) * 0.1
        v1 = jax.random.uniform(ks[6], (C,), dtype=jnp.float32, minval=0.5, maxval=1.5)
        g2 = jax.random.uniform(ks[7], (C,), dtype=jnp.float32, minval=0.5, maxval=1.5)
        b2 = jax.random.normal(ks[8], (C,), dtype=jnp.float32) * 0.1
        m2 = jax.random.normal(ks[9], (C,), dtype=jnp.float32) * 0.1
        v2 = jax.random.uniform(ks[10], (C,), dtype=jnp.float32, minval=0.5, maxval=1.5)
        return {'x': x, 'w1': w1, 'g1': g1, 'b1': b1, 'm1': m1, 'v1': v1, 'w2': w2, 'g2': g2, 'b2': b2, 'm2': m2, 'v2': v2}
    _L0_conv_all = _L0_conv_setup()
    _L0_conv_in = {k: v for k, v in _L0_conv_all.items() if k in ('w1', 'g1', 'b1', 'm1', 'v1', 'w2', 'g2', 'b2', 'm2', 'v2')}
    del _L0_conv_all
    return {'x': x, 'L0_conv_w1': _L0_conv_in['w1'], 'L0_conv_g1': _L0_conv_in['g1'], 'L0_conv_b1': _L0_conv_in['b1'], 'L0_conv_m1': _L0_conv_in['m1'], 'L0_conv_v1': _L0_conv_in['v1'], 'L0_conv_w2': _L0_conv_in['w2'], 'L0_conv_g2': _L0_conv_in['g2'], 'L0_conv_b2': _L0_conv_in['b2'], 'L0_conv_m2': _L0_conv_in['m2'], 'L0_conv_v2': _L0_conv_in['v2']}

def reference(x, L0_conv_w1, L0_conv_g1, L0_conv_b1, L0_conv_m1, L0_conv_v1, L0_conv_w2, L0_conv_g2, L0_conv_b2, L0_conv_m2, L0_conv_v2):
    import jax
    import jax.numpy as jnp

    def _L0_conv_ref(x, w1, g1, b1, m1, v1, w2, g2, b2, m2, v2):
        import jax, jax.numpy as jnp
        import numpy as np
        EPS = 1e-05

        def _conv3x3(x, w, stride=1):
            return jax.lax.conv_general_dilated(x, w, window_strides=(stride, stride), padding=((1, 1), (1, 1)), dimension_numbers=('NCHW', 'OIHW', 'NCHW'))

        def _bn(x, gamma, beta, mean, var):
            inv = gamma * jax.lax.rsqrt(var + EPS)
            return x * inv[None, :, None, None] + (beta - mean * inv)[None, :, None, None]
        identity = x
        out = jax.nn.relu(_bn(_conv3x3(x, w1, stride=1), g1, b1, m1, v1))
        out = _bn(_conv3x3(out, w2, stride=1), g2, b2, m2, v2)
        return jax.nn.relu(out + identity)

    def _gn(v, G=32, eps=1e-05):
        B_, C_, H_, W_ = v.shape
        g = v.reshape(B_, G, C_ // G, H_, W_)
        m = jnp.mean(g, axis=(2, 3, 4), keepdims=True)
        s = jnp.var(g, axis=(2, 3, 4), keepdims=True)
        return ((g - m) / jnp.sqrt(s + eps)).reshape(v.shape)

    def _ln_c(v, eps=1e-06):
        m = jnp.mean(v, axis=1, keepdims=True)
        s = jnp.var(v, axis=1, keepdims=True)
        return (v - m) / jnp.sqrt(s + eps)

    def _ln_t(v, eps=1e-05):
        m = jnp.mean(v, axis=-1, keepdims=True)
        s = jnp.var(v, axis=-1, keepdims=True)
        return (v - m) / jnp.sqrt(s + eps)

    def _to_tokens(v):
        B_, C_, H_, W_ = v.shape
        return v.reshape(B_, C_, H_ * W_).transpose(0, 2, 1)

    def _from_tokens(t, like):
        B_, C_, H_, W_ = like.shape
        return t.transpose(0, 2, 1).reshape(B_, C_, H_, W_)
    x = _L0_conv_ref(x, L0_conv_w1, L0_conv_g1, L0_conv_b1, L0_conv_m1, L0_conv_v1, L0_conv_w2, L0_conv_g2, L0_conv_b2, L0_conv_m2, L0_conv_v2)
    return x

_drawn_inputs = setup_inputs


def setup_inputs(seed=0):
    import zlib

    import numpy as np

    out = dict(_drawn_inputs(seed))
    spreads = {}
    factors = {}
    for name, (base, spread) in spreads.items():
        noise = np.random.default_rng([zlib.crc32(name.encode()), seed]).standard_normal(out[name].shape)
        drawn = base * np.exp(spread * noise) if base else spread * noise
        out[name] = jnp.asarray(drawn.astype(out[name].dtype))
    for name, factor in factors.items():
        out[name] = (out[name] * factor).astype(out[name].dtype)
    return out
```

```python
from contextlib import ExitStack

import concourse.bass as bass
from concourse import mybir

F32 = mybir.dt.float32
F32R = mybir.dt.float32r
ALU = mybir.AluOpType
ACT = mybir.ActivationFunctionType

EPS = 1e-5
XBUFS = 4
T_PLACE = {1: {0: 0, 3: 1, 1: 2, 2: 3}, 2: {3: 0, 0: 1, 1: 2, 2: 3}}
SUM_BANK = {0: 0, 3: 1, 1: 2, 2: 3}
SUM_ORDER = (1, 2, 0, 3)


def residual_block(nc, x, w1, g1, b1, m1, v1, w2, g2, b2, m2, v2, out):
    N, C, H, W = x.shape
    P = 2 * C
    NQ = H // 2
    NP = NQ + 1
    WQ = W // 2
    TAPS = 9
    assert P == 128 and N % 4 == 0

    HALF1 = ((0, (NP + 1) // 2), ((NP + 1) // 2, NP))
    HALF2 = ((0, NQ // 2), (NQ // 2, NQ))
    XPART = ((0, HALF1[0][1]), (HALF1[0][1], NQ))
    MAXN = HALF1[0][1] * WQ

    HPLANE = NP * (WQ + 1) + 1

    with ExitStack() as ctx:
        def sb(name, shape, dt=F32):
            return ctx.enter_context(nc.sbuf_tensor(name, shape, dt))

        def sem(name):
            return ctx.enter_context(nc.semaphore(name))

        x_sb = sb("x_sb", [P, XBUFS, NQ, W + 2])
        t_x = sb("t_x", [P, 4, NQ, WQ])
        t_hi = sb("t_hi", [P, 2, 4, NQ + 2, WQ], F32R)
        t_lo = sb("t_lo", [P, 2, 4, NQ + 2, WQ], F32R)
        hidden = sb("hidden", [P, 2 * (HPLANE + 1)])
        t_h = sb("t_h", [P, 2, 4, NP, WQ])
        z = sb("z", [P, 2, MAXN])
        uv = sb("uv", [P, 2, 2, MAXN])
        y1 = sb("y1", [P, 2, 2, MAXN])
        y2 = sb("y2", [P, 2, NQ // 2, W])
        w_raw = {1: sb("w1_raw", [P, 3, 3, C]), 2: sb("w2_raw", [P, 3, 3, C])}
        gam = sb("gam", [P, 2 * C + 2])
        var = sb("var", [P, 2 * C + 2])
        inv = sb("inv", [P, 2 * C + 2])
        tmp = sb("tmp", [P, 2 * C + 2])
        beta = sb("beta", [P, 2])
        mean = sb("mean", [P, 2])
        bias = sb("bias", [P, 2])
        g_t = {1: sb("g1_t", [P, 4, 3, C]), 2: sb("g2_t", [P, 4, 3, C])}
        g_sum = {1: sb("g1_sum", [P, 3, C]), 2: sb("g2_sum", [P, 3, C])}
        wmat = {1: sb("w1_mat", [P, 4, 2, P]), 2: sb("w2_mat", [P, 4, 2, P])}
        w1_hi = sb("w1_hi", [P, 4, 2, P], F32R)
        w1_lo = sb("w1_lo", [P, 4, 2, P], F32R)

        psum = ctx.enter_context(nc.psum_tensor("psum", [P, 2, 4, 512], F32))

        x_in = [sem(f"x_in{i}") for i in range(XBUFS)]
        w_in = {1: sem("w1_in"), 2: sem("w2_in")}
        bn_in = sem("bn_in")
        zeroed = sem("zeroed")
        var_eps = sem("var_eps")
        std_ready = sem("std_ready")
        bn_ready = sem("bn_ready")
        w_ready = {1: sem("w1_ready"), 2: sem("w2_ready")}
        prep = {1: sem("prep1"), 2: sem("prep2")}
        tx_ready = sem("tx_ready")
        hi_ready = sem("hi_ready")
        lo_ready = sem("lo_ready")
        hidden_ready = sem("hidden_ready")
        th_ready = sem("th_ready")
        sums = {1: sem("sums1"), 2: sem("sums2")}
        z_ready = {1: sem("z1_ready"), 2: sem("z2_ready")}
        uv_ready = {1: sem("uv1_ready"), 2: sem("uv2_ready")}
        y_ready = {1: sem("y1_ready"), 2: sem("y2_ready")}
        res_ready = sem("res_ready")
        out_ready = sem("out_ready")
        stored = [sem("stored_a"), sem("stored_b")]

        x_rows = x.rearrange("n c (j p) w -> n p c j w", p=2)
        out_rows = out.rearrange("n c (j p) w -> n p c j w", p=2)

        hid_data = hidden[:, 0:2 * (HPLANE + 1)].rearrange("p (s r) -> p s r", s=2)[:, :, 0:NP * (WQ + 1)] \
            .rearrange("p s (r c) -> p s r c", c=WQ + 1)
        hid_cols = hidden[:, 0:2 * HPLANE].rearrange("p (s r) -> p s r", s=2)[:, :, 0:NP * (WQ + 1)] \
            .rearrange("p s (r c) -> p s r c", c=WQ + 1)

        def wait(eng, semaphore, value):
            if isinstance(value, int) and value <= 0:
                return
            eng.wait_ge(semaphore, value)

        def run(eng, step):
            for s in (-1, 0, 1):
                step(s, s % 4)
            with eng.Fori(0, (N - 4) // 4) as turn:
                for k in range(4):
                    step(turn * 4 + (2 + k), (2 + k) % 4)
            for s in range(N - 2, N + 2):
                step(s, s % 4)

        def there_is(s, image):
            return not isinstance(s, int) or 0 <= image < N

        X_BLOCKS = ((0, 0, 1, 0), (0, 1, 0, 0), (0, 1, 1, 1), (1, 0, 0, 1), (1, 0, 1, 2), (1, 1, 0, 2))
        HID_BLOCKS = ((0, 0, 0, 1), (0, 0, 1, 0), (0, 1, 0, 0), (1, 0, 1, 2), (1, 1, 0, 2), (1, 1, 1, 1))

        def prepare_weights(eng, conv, blocks):
            done = [0]

            def after(ins):
                done[0] += 1
                ins.then_inc(prep[conv], 1)
                eng.wait_ge(prep[conv], done[0])

            w, g, total, mat = w_raw[conv], g_t[conv], g_sum[conv], wmat[conv]
            after(eng.memset(mat[:], 0.0))
            eng.wait_ge(w_in[conv], 32)
            eng.wait_ge(bn_ready, 1)
            c0 = (conv - 1) * C
            scale = inv[:, c0:c0 + C].unsqueeze(1).broadcast_to((P, TAPS, C))
            flat = w[:].rearrange("p a b c -> p (a b) c")
            after(eng.tensor_tensor(flat, flat, scale, ALU.mult))
            after(eng.tensor_tensor(total[:], w[:, :, 0, :], w[:, :, 2, :], ALU.add))
            after(eng.tensor_tensor(g[:, 1], total[:], w[:, :, 1, :], ALU.add))
            after(eng.tensor_tensor(g[:, 2], total[:], w[:, :, 1, :], ALU.subtract))
            after(eng.tensor_scalar(g[:, 1:3], g[:, 1:3], 0.5, None, ALU.mult))
            after(eng.tensor_copy(g[:, 0], w[:, :, 0, :]))
            after(eng.tensor_scalar(g[:, 3], w[:, :, 2, :], -1.0, None, ALU.mult))
            for far, ki, mo, kh in blocks:
                half = slice(ki * C, ki * C + C)
                after(eng.tensor_copy(mat[half, :, far, mo * C:mo * C + C], g[half, :, kh, :]))
            if conv == 1:
                after(eng.tensor_copy(w1_hi[:], mat[:]))
                after(eng.tensor_tensor(w1_lo[:], mat[:], w1_hi[:].bitcast(F32), ALU.subtract))
            eng.memset(total[:], 0.0).then_inc(w_ready[conv], 1)

        block = ctx.enter_context(nc.Block())

        @block.sync
        def _(sp):
            def load(n, k):
                if isinstance(n, int) and n >= N:
                    return
                wait(sp, res_ready, 2 * (n - XBUFS) + 2)
                for parity in range(2):
                    sp.dma_start(x_sb[parity * C:parity * C + C, k, :, 1:W + 1],
                                 x_rows[n, parity]).then_inc(x_in[k], 16)

            def store(n, half):
                j0, j1 = HALF2[half]
                wait(sp, out_ready, 2 * n + half + 1)
                for parity in range(2):
                    sp.dma_start(out_rows[n, parity][:, j0:j1, :],
                                 y2[parity * C:parity * C + C, half]).then_inc(stored[half], 16)

            load(0, 0)
            for parity in range(2):
                half = slice(parity * C, parity * C + C)
                for tile, rows in ((gam, (g1, g2)), (var, (v1, v2))):
                    for i, row in enumerate(rows):
                        sp.dma_start(tile[half, i * C:i * C + C], row.partition_broadcast(C)).then_inc(bn_in, 16)
                        sp.dma_start(tile[half, 2 * C + i:2 * C + i + 1], row.unsqueeze(1)).then_inc(bn_in, 16)
                for tile, rows in ((beta, (b1, b2)), (mean, (m1, m2))):
                    for i, row in enumerate(rows):
                        sp.dma_start(tile[half, i:i + 1], row.unsqueeze(1)).then_inc(bn_in, 16)
                sp.dma_start(w_raw[1][half], w1).then_inc(w_in[1], 16)
            for parity in range(2):
                sp.dma_start(w_raw[2][parity * C:parity * C + C], w2).then_inc(w_in[2], 16)

            def step(s, k):
                if not isinstance(s, int) or s + 2 < N:
                    load(s + 2, (k + 2) % XBUFS)
                if there_is(s, s - 2):
                    store(s - 2, 1)
                if there_is(s, s - 1):
                    store(s - 1, 0)

            run(sp, step)
            for half in range(2):
                sp.wait_ge(stored[half], 32 * N)

        @block.gpsimd
        def _(pool):
            for t in (t_hi, t_lo):
                for b in range(2):
                    for row in (0, NQ + 1):
                        nc.gpsimd.memset(t[:, b, :, row, :].bitcast(F32), 0.0).then_inc(zeroed, 1)
            prepare_weights(pool, 2, HID_BLOCKS)

            def residual(n, k, half):
                j0, j1 = HALF2[half]
                pool.wait_ge(y_ready[2], 2 * n + half + 1)
                nc.gpsimd.tensor_tensor(y2[:, half], y2[:, half], x_sb[:, k, j0:j1, 1:W + 1],
                                        ALU.add).then_inc(res_ready, 1)

            def step(s, k):
                if there_is(s, s - 2):
                    residual(s - 2, (k + 2) % XBUFS, 1)
                if there_is(s, s - 1):
                    residual(s - 1, (k + 3) % XBUFS, 0)

            run(pool, step)

        @block.vector
        def _(dve):
            nc.vector.memset(x_sb[:, :, :, 0:1], 0.0)
            nc.vector.memset(x_sb[:, :, :, W + 1:W + 2], 0.0)
            nc.vector.memset(hidden[:], 0.0).then_inc(zeroed, 1)

            bn = [0]

            def after(ins):
                bn[0] += 1
                ins.then_inc(var_eps, 1)
                dve.wait_ge(var_eps, bn[0])

            dve.wait_ge(bn_in, 16 * 24)
            after(nc.vector.tensor_scalar(var[:], var[:], EPS, None, ALU.add))
            dve.wait_ge(std_ready, 1)
            after(nc.vector.reciprocal(inv[:], inv[:]))
            after(nc.vector.tensor_tensor(tmp[:], inv[:], inv[:], ALU.mult))
            after(nc.vector.tensor_tensor(tmp[:], tmp[:], var[:], ALU.mult))
            after(nc.vector.tensor_scalar(tmp[:], tmp[:], -0.5, 1.5, ALU.mult, ALU.add))
            after(nc.vector.tensor_tensor(inv[:], inv[:], tmp[:], ALU.mult))
            after(nc.vector.tensor_tensor(inv[:], inv[:], gam[:], ALU.mult))
            after(nc.vector.tensor_tensor(bias[:], mean[:], inv[:, 2 * C:2 * C + 2], ALU.mult))
            nc.vector.tensor_tensor(bias[:], beta[:], bias[:], ALU.subtract).then_inc(bn_ready, 1)
            prepare_weights(dve, 1, X_BLOCKS)

            def transform_x(n, k, part):
                j0, j1 = XPART[part]
                rows = x_sb[:, k, j0:j1, :]
                if part == 0:
                    dve.wait_ge(x_in[k], (n - k) * (32 // XBUFS) + 32)
                wait(dve, lo_ready, 2 * (n - 1) + part + 1)
                nc.vector.tensor_tensor(t_x[:, 0:2, j0:j1, :].rearrange("p s j q -> p j q s"),
                                        rows[:, :, 0:W].rearrange("p j (q s) -> p j q s", s=2),
                                        rows[:, :, 2:W + 2].rearrange("p j (q s) -> p j q s", s=2),
                                        ALU.subtract)
                even = rows[:, :, 1:W + 1].rearrange("p j (q s) -> p j q s", s=2)[:, :, :, 0]
                odd = rows[:, :, 1:W + 1].rearrange("p j (q s) -> p j q s", s=2)[:, :, :, 1]
                nc.vector.tensor_tensor(t_x[:, 2, j0:j1, :], even, odd, ALU.add)
                nc.vector.tensor_tensor(t_x[:, 3, j0:j1, :], odd, even, ALU.subtract).then_inc(tx_ready, 1)

            def split_x(n, b, part):
                j0, j1 = XPART[part]
                dve.wait_ge(hi_ready, 2 * n + part + 1)
                flat = t_x[:, :, j0:j1, :].rearrange("p s j q -> p s (j q)")
                hi = t_hi[:, b, :, j0 + 1:j1 + 1, :].rearrange("p s j q -> p s (j q)").bitcast(F32)
                lo = t_lo[:, b, :, j0 + 1:j1 + 1, :].rearrange("p s j q -> p s (j q)")
                nc.vector.tensor_tensor(lo, flat, hi, ALU.subtract).then_inc(lo_ready, 1)

            def join(conv, n, half):
                r0, r1 = (HALF1, HALF2)[conv - 1][half]
                width = (r1 - r0) * WQ
                bank = psum[:, half]
                dve.wait_ge(z_ready[conv], 2 * n + half + 1)
                dve.wait_ge(sums[conv], 4 * (2 * n + half) + 2)
                nc.vector.tensor_tensor(uv[:, half, 0, 0:width], z[:, half, 0:width],
                                        bank[:, SUM_BANK[2], 0:width], ALU.add)
                nc.vector.tensor_tensor(uv[:, half, 1, 0:width], z[:, half, 0:width],
                                        bank[:, SUM_BANK[2], 0:width], ALU.subtract) \
                    .then_inc(uv_ready[conv], 1)
                dve.wait_ge(sums[conv], 4 * (2 * n + half) + 4)
                dve.wait_ge(uv_ready[conv], 2 * n + half + 1)
                if conv == 1:
                    wait(dve, hidden_ready, 2 * (n - 1) + half + 1)
                    nc.vector.tensor_tensor(y1[:, half, :, 0:width], uv[:, half, :, 0:width],
                                            bank[:, 0:2, 0:width], ALU.add).then_inc(y_ready[1], 1)
                else:
                    wait(dve, stored[half], 32 * n)
                    nc.vector.tensor_tensor(
                        y2[:, half].rearrange("p j (q s) -> p s j q", s=2),
                        uv[:, half, :, 0:width].rearrange("p s (j q) -> p s j q", q=WQ),
                        bank[:, 0:2, 0:width].rearrange("p s (j q) -> p s j q", q=WQ),
                        ALU.add).then_inc(y_ready[2], 1)

            def transform_hidden(n, b, half):
                k0, k1 = HALF1[half]
                dve.wait_ge(hidden_ready, 2 * n + half + 1)
                wait(dve, sums[2], 8 * (n - 1))
                cols = hid_cols[:, :, k0:k1, :]
                nc.vector.tensor_tensor(t_h[:, b, 0:2, k0:k1, :], cols[:, :, :, 0:WQ], cols[:, :, :, 1:WQ + 1],
                                        ALU.subtract)
                even = hid_data[:, 0, k0:k1, 0:WQ]
                odd = hid_data[:, 1, k0:k1, 0:WQ]
                nc.vector.tensor_tensor(t_h[:, b, 2, k0:k1, :], even, odd, ALU.add)
                nc.vector.tensor_tensor(t_h[:, b, 3, k0:k1, :], odd, even, ALU.subtract).then_inc(th_ready, 1)

            def step(s, k):
                if there_is(s, s - 2):
                    join(2, s - 2, 1)
                if there_is(s, s + 1):
                    transform_x(s + 1, (k + 1) % XBUFS, 0)
                if there_is(s, s):
                    join(1, s, 0)
                if there_is(s, s + 1):
                    transform_x(s + 1, (k + 1) % XBUFS, 1)
                if there_is(s, s):
                    join(1, s, 1)
                if there_is(s, s + 1):
                    split_x(s + 1, (k + 1) % 2, 0)
                if there_is(s, s):
                    transform_hidden(s, k % 2, 0)
                if there_is(s, s - 1):
                    join(2, s - 1, 0)
                if there_is(s, s + 1):
                    split_x(s + 1, (k + 1) % 2, 1)
                if there_is(s, s):
                    transform_hidden(s, k % 2, 1)

            run(dve, step)

        @block.scalar
        def _(act):
            act.wait_ge(var_eps, 1)
            nc.scalar.activation(inv[:], var[:], ACT.Sqrt).then_inc(std_ready, 1)

            def high_part(n, b, part):
                j0, j1 = XPART[part]
                act.wait_ge(tx_ready, 2 * n + part + 1)
                wait(act, sums[1], 8 * (n - 1))
                flat = t_x[:, :, j0:j1, :].rearrange("p s j q -> p s (j q)")
                hi = t_hi[:, b, :, j0 + 1:j1 + 1, :].rearrange("p s j q -> p s (j q)")
                nc.scalar.activation(hi, flat, ACT.Copy).then_inc(hi_ready, 1)

            def copy_sum(conv, n, half):
                r0, r1 = (HALF1, HALF2)[conv - 1][half]
                width = (r1 - r0) * WQ
                if conv == 1 and isinstance(n, int) and n == 0 and half == 0:
                    act.wait_ge(bn_ready, 1)
                act.wait_ge(sums[conv], 4 * (2 * n + half) + 1)
                nc.scalar.activation(z[:, half, 0:width], psum[:, half, SUM_BANK[1], 0:width], ACT.Identity,
                                     bias=bias[:, conv - 1:conv]).then_inc(z_ready[conv], 1)

            def relu_hidden(n, half):
                k0, k1 = HALF1[half]
                act.wait_ge(y_ready[1], 2 * n + half + 1)
                wait(act, th_ready, 2 * (n - 1) + half + 1)
                src = y1[:, half, :, 0:(k1 - k0) * WQ].rearrange("p s (r q) -> p s r q", q=WQ)
                if half == 0:
                    nc.scalar.activation(hid_data[0:C, :, 0, 0:WQ], src[0:C, :, 0, :], ACT.Relu)
                    nc.scalar.activation(hid_data[:, :, 1:k1, 0:WQ], src[:, :, 1:, :], ACT.Relu) \
                        .then_inc(hidden_ready, 1)
                else:
                    last = k1 - k0 - 1
                    nc.scalar.activation(hid_data[C:P, :, NP - 1, 0:WQ], src[C:P, :, last, :], ACT.Relu)
                    nc.scalar.activation(hid_data[:, :, k0:NP - 1, 0:WQ], src[:, :, 0:last, :], ACT.Relu) \
                        .then_inc(hidden_ready, 1)

            def relu_out(n, half):
                act.wait_ge(res_ready, 2 * n + half + 1)
                nc.scalar.activation(y2[:, half], y2[:, half], ACT.Relu).then_inc(out_ready, 1)

            def step(s, k):
                if there_is(s, s):
                    copy_sum(1, s, 0)
                if there_is(s, s + 1):
                    high_part(s + 1, (k + 1) % 2, 0)
                if there_is(s, s - 2):
                    relu_out(s - 2, 1)
                if there_is(s, s):
                    copy_sum(1, s, 1)
                    if isinstance(s, int) and s == 0:
                        act.wait_ge(zeroed, 9)
                    relu_hidden(s, 0)
                if there_is(s, s + 1):
                    high_part(s + 1, (k + 1) % 2, 1)
                if there_is(s, s):
                    relu_hidden(s, 1)
                if there_is(s, s - 1):
                    copy_sum(2, s - 1, 0)
                    copy_sum(2, s - 1, 1)
                    relu_out(s - 1, 0)

            run(act, step)

        @block.tensor
        def _(pe):
            def sum_products(conv, n, b, half, passes, rows):
                r0, r1 = (HALF1, HALF2)[conv - 1][half]
                width = (r1 - r0) * WQ
                for i in SUM_ORDER:
                    place = T_PLACE[conv][i]
                    todo = [(far, t, w) for far in range(2) for t, w in passes]
                    for at, (far, t, w) in enumerate(todo):
                        moving = t[:, b, place, r0 + far:r1 + far, :].rearrange("p r q -> p (r q)")
                        last = nc.tensor.matmul(psum[:, half, SUM_BANK[i], 0:width], w[:, i, far, :], moving,
                                                start=at == 0, stop=at == len(todo) - 1)
                    last.then_inc(sums[conv], 1)

            def conv1(n, b, half):
                pe.wait_ge(lo_ready, 2 * n + half + 1)
                wait(pe, y_ready[2], 2 * (n - 2) + half + 1)
                sum_products(1, n, b, half, ((t_hi, w1_hi), (t_lo, w1_hi), (t_hi, w1_lo)), NQ)

            def conv2(n, b, half, next_exists):
                pe.wait_ge(th_ready, 2 * n + half + 1)
                if next_exists:
                    wait(pe, y_ready[1], 2 * (n + 1) + half + 1)
                else:
                    wait(pe, y_ready[2], 2 * (n - 1) + half + 1)
                sum_products(2, n, b, half, ((t_h, wmat[2]),), NP)

            pe.wait_ge(zeroed, 9)
            pe.wait_ge(w_ready[1], 1)

            def step(s, k):
                if there_is(s, s):
                    conv1(s, k % 2, 0)
                    conv1(s, k % 2, 1)
                if isinstance(s, int) and s == 1:
                    pe.wait_ge(w_ready[2], 1)
                if there_is(s, s - 1):
                    exists = not isinstance(s, int) or s < N
                    conv2(s - 1, (k + 1) % 2, 0, exists)
                    conv2(s - 1, (k + 1) % 2, 1, exists)

            run(pe, step)


_PARAMS = ["g1", "b1", "m1", "v1"], ["g2", "b2", "m2", "v2"]


def kernel(**inputs):
    import numpy as np
    import concourse.bacc as bacc
    from concourse.bass_utils import run_bass_kernel_spmd

    arrays = {"x": np.ascontiguousarray(inputs["x"])}
    for layer in (1, 2):
        arrays[f"w{layer}"] = np.ascontiguousarray(np.transpose(inputs[f"L0_conv_w{layer}"], (1, 2, 3, 0)))
        for name in _PARAMS[layer - 1]:
            arrays[name] = np.ascontiguousarray(inputs[f"L0_conv_{name}"])

    nc = bacc.Bacc("TRN2", target_bir_lowering=False, num_devices=1)
    given = {name: nc.dram_tensor(f"{name}_dram", a.shape, mybir.dt.from_np(a.dtype), kind="ExternalInput").ap()
             for name, a in arrays.items()}
    out = nc.dram_tensor("out_dram", arrays["x"].shape, F32, kind="ExternalOutput").ap()
    residual_block(nc, given["x"], given["w1"], given["g1"], given["b1"], given["m1"], given["v1"],
                   given["w2"], given["g2"], given["b2"], given["m2"], given["v2"], out)
    result = run_bass_kernel_spmd(nc, [{f"{name}_dram": a for name, a in arrays.items()}], core_ids=[0])
    return result.results[0]["out_dram"]
```

```python
from contextlib import ExitStack

import concourse.bass as bass
from concourse import mybir

F32 = mybir.dt.float32
F32R = mybir.dt.float32r
ALU = mybir.AluOpType
ACT = mybir.ActivationFunctionType

EPS = 1e-5
XBUFS = 4
OUTER = {1: {0: 0, 3: 1}, 2: {3: 0, 0: 1}}
INNER = {1: 0, 2: 1}
EVEN, ODD, SUM_T1, SUM_T2 = range(4)


def residual_block(nc, x, w1, w2, gammas, variances, by_channel, out):
    N, C, H, W = x.shape
    P = 2 * C
    NQ = H // 2
    NP = NQ + 1
    WQ = W // 2
    TAPS = 9
    assert P == 128 and N % 4 == 0

    HALF1 = ((0, (NP + 1) // 2), ((NP + 1) // 2, NP))
    HALF2 = ((0, NQ // 2), (NQ // 2, NQ))
    XPART = ((0, HALF1[0][1]), (HALF1[0][1], NQ))
    MAXN = HALF1[0][1] * WQ

    HPLANE = NP * (WQ + 1) + 1

    with ExitStack() as ctx:
        def sb(name, shape, dt=F32):
            return ctx.enter_context(nc.sbuf_tensor(name, shape, dt))

        def sem(name):
            return ctx.enter_context(nc.semaphore(name))

        x_sb = sb("x_sb", [P, XBUFS, NQ, W + 2])
        t_x = sb("t_x", [P, 4, NQ, WQ])
        x_hi = sb("x_hi", [P, 2, 4, NQ + 2, WQ], F32R)
        x_lo = sb("x_lo", [P, 2, 4, NQ + 2, WQ], F32R)
        hidden = sb("hidden", [P, 2 * (HPLANE + 1)])
        t_inner = sb("t_inner", [P, 2, 2, NP, WQ])
        t_outer = sb("t_outer", [P, 2, NP, WQ])
        h_hi = sb("h_hi", [P, 2, 2, NP, WQ], F32R)
        h_lo = sb("h_lo", [P, 2, 2, NP, WQ], F32R)
        z = sb("z", [P, 2, 2, MAXN])
        out_sb = sb("out_sb", [P, 2, NQ // 2, W])
        w_raw = {1: sb("w1_raw", [P, 3, 3, C]), 2: sb("w2_raw", [P, 3, 3, C])}
        gam = sb("gam", [P, 2 * C + 2])
        var = sb("var", [P, 2 * C + 2])
        inv = sb("inv", [P, 2 * C + 2])
        tmp = sb("tmp", [P, 2 * C + 2])
        bn_cols = sb("bn_cols", [P, 4, 2])
        bias = sb("bias", [P, 2])
        g_t = {1: sb("g1_t", [P, 4, 3, C]), 2: sb("g2_t", [P, 4, 3, C])}
        g_sum = {1: sb("g1_sum", [P, 3, C]), 2: sb("g2_sum", [P, 3, C])}
        wmat = {1: sb("w1_mat", [P, 4, 2, P]), 2: sb("w2_mat", [P, 4, 2, P])}
        w_hi = {1: sb("w1_hi", [P, 4, 2, P], F32R), 2: sb("w2_hi", [P, 4, 2, P], F32R)}
        w_lo = {1: sb("w1_lo", [P, 4, 2, P], F32R), 2: sb("w2_lo", [P, 4, 2, P], F32R)}

        psum = ctx.enter_context(nc.psum_tensor("psum", [P, 2, 4, 512], F32))

        x_in = [sem(f"x_in{i}") for i in range(XBUFS)]
        w_in = {1: sem("w1_in"), 2: sem("w2_in")}
        bn_in = sem("bn_in")
        zeroed = sem("zeroed")
        bits_set = sem("bits_set")
        bn_step = sem("bn_step")
        std_ready = sem("std_ready")
        bn_ready = sem("bn_ready")
        w_ready = {1: sem("w1_ready"), 2: sem("w2_ready")}
        prep = {1: sem("prep1"), 2: sem("prep2")}
        tx_ready = sem("tx_ready")
        xhi_ready = sem("xhi_ready")
        xlo_ready = sem("xlo_ready")
        th_ready = sem("th_ready")
        hhi_ready = sem("hhi_ready")
        hlo_ready = sem("hlo_ready")
        inner = {1: sem("inner1"), 2: sem("inner2")}
        z_ready = {1: sem("z1_ready"), 2: sem("z2_ready")}
        res_ready = sem("res_ready")
        joined = {1: sem("joined1"), 2: sem("joined2")}
        outer = {1: sem("outer1"), 2: sem("outer2")}
        hidden_ready = sem("hidden_ready")
        out_ready = sem("out_ready")
        stored = [sem("stored_a"), sem("stored_b")]

        x_rows = x.rearrange("n c (j p) w -> n p c j w", p=2)
        out_rows = out.rearrange("n c (j p) w -> n p c j w", p=2)

        hid_data = hidden[:, 0:2 * (HPLANE + 1)].rearrange("p (s r) -> p s r", s=2)[:, :, 0:NP * (WQ + 1)] \
            .rearrange("p s (r c) -> p s r c", c=WQ + 1)
        hid_cols = hidden[:, 0:2 * HPLANE].rearrange("p (s r) -> p s r", s=2)[:, :, 0:NP * (WQ + 1)] \
            .rearrange("p s (r c) -> p s r c", c=WQ + 1)

        def wait(eng, semaphore, value):
            if isinstance(value, int) and value <= 0:
                return
            eng.wait_ge(semaphore, value)

        def run(eng, step):
            for s in (-1, 0, 1):
                step(s, s % 4)
            with eng.Fori(0, (N - 4) // 4) as turn:
                for k in range(4):
                    step(turn * 4 + (2 + k), (2 + k) % 4)
            for s in range(N - 2, N + 2):
                step(s, s % 4)

        def there_is(s, image):
            return not isinstance(s, int) or 0 <= image < N

        X_BLOCKS = ((0, 0, 1, 0), (0, 1, 0, 0), (0, 1, 1, 1), (1, 0, 0, 1), (1, 0, 1, 2), (1, 1, 0, 2))
        HID_BLOCKS = ((0, 0, 0, 1), (0, 0, 1, 0), (0, 1, 0, 0), (1, 0, 1, 2), (1, 1, 0, 2), (1, 1, 1, 1))

        def prepare_weights(eng, conv, blocks):
            done = [0]

            def after(ins):
                done[0] += 1
                ins.then_inc(prep[conv], 1)
                eng.wait_ge(prep[conv], done[0])

            w, g, total, mat = w_raw[conv], g_t[conv], g_sum[conv], wmat[conv]
            after(eng.memset(mat[:], 0.0))
            eng.wait_ge(w_in[conv], 32)
            eng.wait_ge(bn_ready, 1)
            c0 = (conv - 1) * C
            scale = inv[:, c0:c0 + C].unsqueeze(1).broadcast_to((P, TAPS, C))
            flat = w[:].rearrange("p a b c -> p (a b) c")
            after(eng.tensor_tensor(flat, flat, scale, ALU.mult))
            after(eng.tensor_tensor(total[:], w[:, :, 0, :], w[:, :, 2, :], ALU.add))
            after(eng.tensor_tensor(g[:, 1], total[:], w[:, :, 1, :], ALU.add))
            after(eng.tensor_tensor(g[:, 2], total[:], w[:, :, 1, :], ALU.subtract))
            after(eng.tensor_scalar(g[:, 1:3], g[:, 1:3], 0.5, None, ALU.mult))
            after(eng.tensor_copy(g[:, 0], w[:, :, 0, :]))
            after(eng.tensor_scalar(g[:, 3], w[:, :, 2, :], -1.0, None, ALU.mult))
            for far, ki, mo, kh in blocks:
                half = slice(ki * C, ki * C + C)
                after(eng.tensor_copy(mat[half, :, far, mo * C:mo * C + C], g[half, :, kh, :]))
            after(eng.tensor_copy(w_hi[conv][:], mat[:]))
            eng.tensor_tensor(w_lo[conv][:], mat[:], w_hi[conv][:].bitcast(F32),
                              ALU.subtract).then_inc(w_ready[conv], 1)

        def before_conv2(n):
            return (2, n - 1) if isinstance(n, int) and n == N - 1 else (1, n + 1)

        def load(eng, n, k):
            wait(eng, res_ready, 2 * (n - XBUFS) + 2)
            for parity in range(2):
                eng.dma_start(x_sb[parity * C:parity * C + C, k, :, 1:W + 1],
                              x_rows[n, parity]).then_inc(x_in[k], 16)

        block = ctx.enter_context(nc.Block())

        @block.sync
        def _(sp):
            def store(n, half):
                j0, j1 = HALF2[half]
                wait(sp, out_ready, 2 * n + half + 1)
                for parity in range(2):
                    sp.dma_start(out_rows[n, parity][:, j0:j1, :],
                                 out_sb[parity * C:parity * C + C, half]).then_inc(stored[half], 16)

            sp.dma_start(gam[:, 0:2 * C], gammas.partition_broadcast(P)).then_inc(bn_in, 16)
            sp.dma_start(var[:, 0:2 * C], variances.partition_broadcast(P)).then_inc(bn_in, 16)
            for parity in range(2):
                half = slice(parity * C, parity * C + C)
                sp.dma_start(bn_cols[half], by_channel).then_inc(bn_in, 16)
                sp.dma_start(w_raw[1][half], w1).then_inc(w_in[1], 16)
            for parity in range(2):
                sp.dma_start(w_raw[2][parity * C:parity * C + C], w2).then_inc(w_in[2], 16)

            def step(s, k):
                if not isinstance(s, int) or s + 2 < N:
                    load(sp, s + 2, (k + 2) % XBUFS)
                if there_is(s, s - 2):
                    store(s - 2, 0)
                    store(s - 2, 1)

            run(sp, step)
            for half in range(2):
                sp.wait_ge(stored[half], 32 * N)

        @block.gpsimd
        def _(pool):
            for t in (x_hi, x_lo):
                for b in range(2):
                    for row in (0, NQ + 1):
                        nc.gpsimd.memset(t[:, b, :, row, :].bitcast(F32), 0.0).then_inc(zeroed, 1)
            prepare_weights(pool, 2, HID_BLOCKS)

            def residual(n, k, half):
                j0, j1 = HALF2[half]
                pool.wait_ge(z_ready[2], 2 * n + half + 1)
                both = z[:, half, :, 0:(j1 - j0) * WQ].rearrange("p s (j q) -> p s j q", q=WQ)
                nc.gpsimd.tensor_tensor(both, both,
                                        x_sb[:, k, j0:j1, 1:W + 1].rearrange("p j (q s) -> p s j q", s=2),
                                        ALU.add).then_inc(res_ready, 1)

            def step(s, k):
                if there_is(s, s - 1):
                    residual(s - 1, (k + 3) % XBUFS, 0)
                    residual(s - 1, (k + 3) % XBUFS, 1)

            run(pool, step)

        @block.vector
        def _(dve):
            nc.vector.memset(x_sb[:, :, :, 0:1], 0.0)
            nc.vector.memset(x_sb[:, :, :, W + 1:W + 2], 0.0)
            nc.vector.memset(hidden[:], 0.0).then_inc(zeroed, 1)

            done = [0]

            def after(ins):
                done[0] += 1
                ins.then_inc(bn_step, 1)
                dve.wait_ge(bn_step, done[0])

            dve.wait_ge(bn_in, 16 * 4)
            nc.vector.tensor_copy(gam[:, 2 * C:], bn_cols[:, 0, :])
            after(nc.vector.tensor_copy(var[:, 2 * C:], bn_cols[:, 1, :]))
            after(nc.vector.tensor_scalar(var[:], var[:], EPS, None, ALU.add))
            dve.wait_ge(std_ready, 1)
            after(nc.vector.reciprocal(inv[:], inv[:]))
            after(nc.vector.tensor_tensor(tmp[:], inv[:], inv[:], ALU.mult))
            after(nc.vector.tensor_tensor(tmp[:], tmp[:], var[:], ALU.mult))
            after(nc.vector.tensor_scalar(tmp[:], tmp[:], -0.5, 1.5, ALU.mult, ALU.add))
            after(nc.vector.tensor_tensor(inv[:], inv[:], tmp[:], ALU.mult))
            after(nc.vector.tensor_tensor(inv[:], inv[:], gam[:], ALU.mult))
            after(nc.vector.tensor_tensor(bias[:], bn_cols[:, 3, :], inv[:, 2 * C:2 * C + 2], ALU.mult))
            nc.vector.tensor_tensor(bias[:], bn_cols[:, 2, :], bias[:], ALU.subtract).then_inc(bn_ready, 1)
            prepare_weights(dve, 1, X_BLOCKS)

            def transform_x(n, k, part):
                j0, j1 = XPART[part]
                rows = x_sb[:, k, j0:j1, :]
                if part == 0:
                    dve.wait_ge(x_in[k], (n - k) * (32 // XBUFS) + 32)
                wait(dve, xlo_ready, 2 * (n - 1) + part + 1)
                nc.vector.tensor_tensor(t_x[:, 0:2, j0:j1, :].rearrange("p s j q -> p j q s"),
                                        rows[:, :, 0:W].rearrange("p j (q s) -> p j q s", s=2),
                                        rows[:, :, 2:W + 2].rearrange("p j (q s) -> p j q s", s=2),
                                        ALU.subtract)
                even = rows[:, :, 1:W + 1].rearrange("p j (q s) -> p j q s", s=2)[:, :, :, 0]
                odd = rows[:, :, 1:W + 1].rearrange("p j (q s) -> p j q s", s=2)[:, :, :, 1]
                nc.vector.tensor_tensor(t_x[:, 2, j0:j1, :], even, odd, ALU.add)
                nc.vector.tensor_tensor(t_x[:, 3, j0:j1, :], odd, even, ALU.subtract).then_inc(tx_ready, 1)

            def split_x(n, b, part):
                j0, j1 = XPART[part]
                dve.wait_ge(xhi_ready, 2 * n + part + 1)
                nc.vector.tensor_tensor(x_lo[:, b, :, j0 + 1:j1 + 1, :].rearrange("p s j q -> p s (j q)"),
                                        t_x[:, :, j0:j1, :].rearrange("p s j q -> p s (j q)"),
                                        x_hi[:, b, :, j0 + 1:j1 + 1, :].rearrange("p s j q -> p s (j q)")
                                        .bitcast(F32), ALU.subtract).then_inc(xlo_ready, 1)

            def join(conv, n, half, before):
                r0, r1 = (HALF1, HALF2)[conv - 1][half]
                width = (r1 - r0) * WQ
                dve.wait_ge(z_ready[1] if conv == 1 else res_ready, 2 * n + half + 1)
                dve.wait_ge(inner[conv], 2 * (2 * n + half) + 2)
                wait(dve, *((hidden_ready if before[0] == 1 else out_ready), 2 * before[1] + half + 1))
                t1 = psum[:, half, SUM_T1, 0:width].unsqueeze(1).broadcast_to((P, 2, width))
                nc.vector.tensor_tensor(psum[:, half, EVEN:ODD + 1, 0:width], t1, z[:, half, :, 0:width],
                                        ALU.add).then_inc(joined[conv], 1)

            def transform_hidden(n, b, half):
                k0, k1 = HALF1[half]
                dve.wait_ge(hidden_ready, 2 * n + half + 1)
                wait(dve, hlo_ready, 2 * (n - 1) + half + 1)
                cols = hid_cols[:, :, k0:k1, :]
                nc.vector.tensor_tensor(t_outer[:, :, k0:k1, :], cols[:, :, :, 0:WQ], cols[:, :, :, 1:WQ + 1],
                                        ALU.subtract)
                even = hid_data[:, 0, k0:k1, 0:WQ]
                odd = hid_data[:, 1, k0:k1, 0:WQ]
                wait(dve, inner[2], 4 * (n - 1))
                nc.vector.tensor_tensor(t_inner[:, b, 0, k0:k1, :], even, odd, ALU.add)
                nc.vector.tensor_tensor(t_inner[:, b, 1, k0:k1, :], odd, even, ALU.subtract) \
                    .then_inc(th_ready, 1)

            def split_hidden(n, b, half):
                k0, k1 = HALF1[half]
                dve.wait_ge(hhi_ready, 2 * n + half + 1)
                nc.vector.tensor_tensor(h_lo[:, b, :, k0:k1, :].rearrange("p s k q -> p s (k q)"),
                                        t_outer[:, :, k0:k1, :].rearrange("p s k q -> p s (k q)"),
                                        h_hi[:, b, :, k0:k1, :].rearrange("p s k q -> p s (k q)")
                                        .bitcast(F32), ALU.subtract).then_inc(hlo_ready, 1)

            def step(s, k):
                ahead, now, last = there_is(s, s + 1), there_is(s, s), there_is(s, s - 1)
                if ahead:
                    transform_x(s + 1, (k + 1) % XBUFS, 0)
                if last:
                    split_hidden(s - 1, (k + 1) % 2, 0)
                if there_is(s, s - 2):
                    join(2, s - 2, 1, before_conv2(s - 2))
                if last:
                    transform_hidden(s - 1, (k + 1) % 2, 1)
                if now:
                    join(1, s, 0, (2, s - 2))
                if last:
                    split_hidden(s - 1, (k + 1) % 2, 1)
                if ahead:
                    transform_x(s + 1, (k + 1) % XBUFS, 1)
                    split_x(s + 1, (k + 1) % 2, 0)
                if now:
                    join(1, s, 1, (2, s - 2))
                if ahead:
                    split_x(s + 1, (k + 1) % 2, 1)
                if last:
                    join(2, s - 1, 0, before_conv2(s - 1))
                if now:
                    transform_hidden(s, k % 2, 0)

            run(dve, step)

        @block.scalar
        def _(act):
            load(act, 0, 0)
            act.wait_ge(bn_step, 2)
            nc.scalar.activation(inv[:], var[:], ACT.Sqrt).then_inc(std_ready, 1)

            def high_x(n, b, part):
                j0, j1 = XPART[part]
                act.wait_ge(tx_ready, 2 * n + part + 1)
                wait(act, outer[1], 2 * (n - 1))
                nc.scalar.activation(x_hi[:, b, :, j0 + 1:j1 + 1, :].rearrange("p s j q -> p s (j q)"),
                                     t_x[:, :, j0:j1, :].rearrange("p s j q -> p s (j q)"),
                                     ACT.Copy).then_inc(xhi_ready, 1)

            def high_hidden(n, b, half):
                k0, k1 = HALF1[half]
                act.wait_ge(th_ready, 2 * n + half + 1)
                wait(act, outer[2], 2 * (n - 1))
                nc.scalar.activation(h_hi[:, b, :, k0:k1, :].rearrange("p s k q -> p s (k q)"),
                                     t_outer[:, :, k0:k1, :].rearrange("p s k q -> p s (k q)"),
                                     ACT.Copy).then_inc(hhi_ready, 1)

            def copy_sum(conv, n, half):
                r0, r1 = (HALF1, HALF2)[conv - 1][half]
                width = (r1 - r0) * WQ
                act.wait_ge(inner[conv], 2 * (2 * n + half) + 1)
                t2 = psum[:, half, SUM_T2, 0:width]
                nc.scalar.activation(z[:, half, 0, 0:width], t2, ACT.Identity, bias=bias[:, conv - 1:conv])
                nc.scalar.activation(z[:, half, 1, 0:width], t2, ACT.Identity, bias=bias[:, conv - 1:conv],
                                     scale=-1.0).then_inc(z_ready[conv], 1)

            def relu_hidden(n, half):
                k0, k1 = HALF1[half]
                act.wait_ge(outer[1], 2 * n + half + 1)
                wait(act, th_ready, 2 * (n - 1) + half + 1)
                src = psum[:, half, EVEN:ODD + 1, 0:(k1 - k0) * WQ].rearrange("p s (r q) -> p s r q", q=WQ)
                if half == 0:
                    nc.scalar.activation(hid_data[0:C, :, 0, 0:WQ], src[0:C, :, 0, :], ACT.Relu)
                    nc.scalar.activation(hid_data[:, :, 1:k1, 0:WQ], src[:, :, 1:, :], ACT.Relu) \
                        .then_inc(hidden_ready, 1)
                else:
                    end = k1 - k0 - 1
                    nc.scalar.activation(hid_data[C:P, :, NP - 1, 0:WQ], src[C:P, :, end, :], ACT.Relu)
                    nc.scalar.activation(hid_data[:, :, k0:NP - 1, 0:WQ], src[:, :, 0:end, :], ACT.Relu) \
                        .then_inc(hidden_ready, 1)

            def relu_out(n, half):
                j0, j1 = HALF2[half]
                act.wait_ge(outer[2], 2 * n + half + 1)
                wait(act, stored[half], 32 * n)
                nc.scalar.activation(
                    out_sb[:, half].rearrange("p j (q s) -> p s j q", s=2),
                    psum[:, half, EVEN:ODD + 1, 0:(j1 - j0) * WQ].rearrange("p s (j q) -> p s j q", q=WQ),
                    ACT.Relu).then_inc(out_ready, 1)

            def step(s, k):
                ahead, now, last = there_is(s, s + 1), there_is(s, s), there_is(s, s - 1)
                if last:
                    relu_hidden(s - 1, 1)
                    high_hidden(s - 1, (k + 1) % 2, 0)
                if ahead:
                    high_x(s + 1, (k + 1) % 2, 0)
                if now:
                    if isinstance(s, int) and s == 0:
                        act.wait_ge(bn_ready, 1)
                        act.wait_ge(zeroed, 9)
                    copy_sum(1, s, 0)
                if there_is(s, s - 2):
                    relu_out(s - 2, 0)
                if last:
                    high_hidden(s - 1, (k + 1) % 2, 1)
                if now:
                    copy_sum(1, s, 1)
                if there_is(s, s - 2):
                    relu_out(s - 2, 1)
                if ahead:
                    high_x(s + 1, (k + 1) % 2, 1)
                if last:
                    copy_sum(2, s - 1, 0)
                if now:
                    relu_hidden(s, 0)
                if last:
                    copy_sum(2, s - 1, 1)

            run(act, step)

        @block.tensor
        def _(pe):
            THREE_PASSES = {1: ((x_hi, w_hi[1]), (x_lo, w_hi[1]), (x_hi, w_lo[1])),
                            2: ((h_hi, w_hi[2]), (h_lo, w_hi[2]), (h_hi, w_lo[2]))}

            def sum_products(conv, b, half, i, place, bank, passes, onto):
                r0, r1 = (HALF1, HALF2)[conv - 1][half]
                width = (r1 - r0) * WQ
                todo = [(far, t, w) for far in range(2) for t, w in passes]
                for at, (far, t, w) in enumerate(todo):
                    moving = t[:, b, place, r0 + far:r1 + far, :].rearrange("p r q -> p (r q)")
                    ins = nc.tensor.matmul(psum[:, half, bank, 0:width], w[:, i, far, :], moving,
                                           start=not onto and at == 0, stop=at == len(todo) - 1,
                                           skip_group_check=onto)
                return ins

            def inner_products(conv, n, b, half, before):
                wait(pe, joined[before[0]], 2 * before[1] + half + 1)
                for i, bank in ((2, SUM_T2), (1, SUM_T1)):
                    if conv == 1:
                        place, passes = 2 + INNER[i], THREE_PASSES[1]
                    else:
                        place, passes = INNER[i], ((t_inner, wmat[2]),)
                    sum_products(conv, b, half, i, place, bank, passes, False).then_inc(inner[conv], 1)

            def outer_products(conv, n, b, half):
                pe.wait_ge(joined[conv], 2 * n + half + 1)
                for i, bank in ((0, EVEN), (3, ODD)):
                    ins = sum_products(conv, b, half, i, OUTER[conv][i], bank, THREE_PASSES[conv], True)
                ins.then_inc(outer[conv], 1)

            pe.wait_ge(zeroed, 9)
            for half in range(2):
                for bank in (EVEN, ODD):
                    nc.tensor.matmul(psum[:, half, bank, 0:MAXN], hidden[:, 0:P], hidden[:, 0:MAXN],
                                     start=True, stop=True).then_inc(bits_set, 1)
            pe.wait_ge(w_ready[1], 1)

            def step(s, k):
                now, last, store = there_is(s, s), there_is(s, s - 1), there_is(s, s - 2)
                for half in range(2):
                    if now:
                        pe.wait_ge(xlo_ready, 2 * s + half + 1)
                        inner_products(1, s, k % 2, half, (2, s - 2))
                    if store:
                        pe.wait_ge(hlo_ready, 2 * (s - 2) + half + 1)
                        outer_products(2, s - 2, k % 2, half)
                if isinstance(s, int) and s == 1:
                    pe.wait_ge(w_ready[2], 1)
                for half in range(2):
                    if last:
                        pe.wait_ge(th_ready, 2 * (s - 1) + half + 1)
                        inner_products(2, s - 1, (k + 1) % 2, half, before_conv2(s - 1))
                    if now:
                        outer_products(1, s, k % 2, half)

            run(pe, step)


def kernel(**inputs):
    import numpy as np
    import concourse.bacc as bacc
    from concourse.bass_utils import run_bass_kernel_spmd

    def both(name):
        return [np.asarray(inputs[f"L0_conv_{name}{layer}"]) for layer in (1, 2)]

    arrays = {"x": np.ascontiguousarray(inputs["x"])}
    for layer in (1, 2):
        arrays[f"w{layer}"] = np.ascontiguousarray(np.transpose(inputs[f"L0_conv_w{layer}"], (1, 2, 3, 0)))
    arrays["gammas"] = np.concatenate(both("g"))
    arrays["variances"] = np.concatenate(both("v"))
    by_channel = np.stack([np.stack(both(name), axis=-1) for name in "gvbm"], axis=1)
    arrays["by_channel"] = np.ascontiguousarray(by_channel)

    nc = bacc.Bacc("TRN2", target_bir_lowering=False, num_devices=1)
    given = {name: nc.dram_tensor(f"{name}_dram", a.shape, mybir.dt.from_np(a.dtype), kind="ExternalInput").ap()
             for name, a in arrays.items()}
    out = nc.dram_tensor("out_dram", arrays["x"].shape, F32, kind="ExternalOutput").ap()
    residual_block(nc, given["x"], given["w1"], given["w2"], given["gammas"], given["variances"],
                   given["by_channel"], out)
    result = run_bass_kernel_spmd(nc, [{f"{name}_dram": a for name, a in arrays.items()}], core_ids=[0])
    return result.results[0]["out_dram"]
```

```python
from contextlib import ExitStack

import concourse.bass as bass
from concourse import mybir

F32 = mybir.dt.float32
F32R = mybir.dt.float32r
ALU = mybir.AluOpType
ACT = mybir.ActivationFunctionType

EPS = 1e-5
XBUFS = 2
TBUFS = 4
OUTER = {1: {0: 0, 3: 1}, 2: {3: 0, 0: 1}}
WARM_UP = 5
EVEN, ODD, SUM_T1, SUM_T2 = range(4)


def residual_block(nc, x, w1, w2, params, out):
    N, C, H, W = x.shape
    P = 2 * C
    NQ = H // 2
    NP = NQ + 1
    WQ = W // 2
    assert P == 128 and N % 4 == 0

    HALF1 = ((0, (NP + 1) // 2), ((NP + 1) // 2, NP))
    HALF2 = ((0, NQ // 2), (NQ // 2, NQ))
    MAXN = HALF1[0][1] * WQ

    HPLANE = NP * (WQ + 1) + 1

    with ExitStack() as ctx:
        def sb(name, shape, dt=F32):
            return ctx.enter_context(nc.sbuf_tensor(name, shape, dt))

        def sem(name):
            return ctx.enter_context(nc.semaphore(name))

        x_sb = sb("x_sb", [P, XBUFS, NQ, W + 2])
        x_outer = sb("x_outer", [P, 2, NQ, WQ])
        x_inner = sb("x_inner", [P, TBUFS, 2, NQ, WQ])
        x_hi = sb("x_hi", [P, 2, 4, NQ + 2, WQ], F32R)
        x_lo = sb("x_lo", [P, 2, 4, NQ + 2, WQ], F32R)
        hidden = sb("hidden", [P, 2 * (HPLANE + 1)])
        t_inner = sb("t_inner", [P, 2, NP, WQ])
        t_outer = sb("t_outer", [P, 2, NP, WQ])
        t1_hi = sb("t1_hi", [P, NP, WQ], F32R)
        t1_lo = sb("t1_lo", [P, NP, WQ], F32R)
        h_hi = sb("h_hi", [P, 2, 2, NP, WQ], F32R)
        h_lo = sb("h_lo", [P, 2, 2, NP, WQ], F32R)
        z = sb("z", [P, 2, 2, MAXN])
        out_sb = sb("out_sb", [P, 2, NQ // 2, W])
        w_raw = {1: sb("w1_raw", [P, 3, 3, C]), 2: sb("w2_raw", [P, 3, 3, C])}
        bn = sb("bn", [P, 8 + 4 * C])
        var = sb("var", [P, 2 + 2 * C])
        inv = sb("inv", [P, 2 + 2 * C])
        tmp = sb("tmp", [P, 2 + 2 * C])
        bias = sb("bias", [P, 2])
        g_t = {1: sb("g1_t", [P, 4, 3, C]), 2: sb("g2_t", [P, 4, 3, C])}
        g_sum = {1: sb("g1_sum", [P, 3, C]), 2: sb("g2_sum", [P, 3, C])}
        wmat = {1: sb("w1_mat", [P, 4, 2, P]), 2: sb("w2_mat", [P, 4, 2, P])}
        w_hi = {1: sb("w1_hi", [P, 4, 2, P], F32R), 2: sb("w2_hi", [P, 4, 2, P], F32R)}
        w_lo = {1: sb("w1_lo", [P, 4, 2, P], F32R), 2: sb("w2_lo", [P, 4, 2, P], F32R)}

        psum = ctx.enter_context(nc.psum_tensor("psum", [P, 2, 4, 512], F32))

        x_in = [sem(f"x_in{i}") for i in range(XBUFS)]
        w_in = {1: sem("w1_in"), 2: sem("w2_in")}
        bn_in = sem("bn_in")
        x_zeroed = sem("x_zeroed")
        mat_zeroed = sem("mat_zeroed")
        zeroed = sem("zeroed")
        bits_set = sem("bits_set")
        var_ready = sem("var_ready")
        std_ready = sem("std_ready")
        inv_ready = sem("inv_ready")
        bn_step = {1: sem("bn_step1"), 2: sem("bn_step2")}
        scale_ready = {1: sem("scale1_ready"), 2: sem("scale2_ready")}
        bias_ready = sem("bias_ready")
        prep = {1: sem("prep1"), 2: sem("prep2")}
        outer_taps = {1: sem("outer_taps1"), 2: sem("outer_taps2")}
        sets = ("inner1", "outer1", "all2")
        mat_filled, mat_ready, whi_ready, wlo_ready = (
            {which: sem(f"{what}_{which}") for which in sets} for what in ("filled", "mat", "whi", "wlo"))
        tx_ready = {"inner": sem("tx_inner"), "outer": sem("tx_outer")}
        xhi_ready = {"inner": sem("xhi_inner"), "outer": sem("xhi_outer")}
        xlo_ready = {"inner": sem("xlo_inner"), "outer": sem("xlo_outer")}
        th_ready = {"t1": sem("th_t1"), "t2": sem("th_t2"), "outer": sem("th_outer")}
        hhi_ready = {"t1": sem("hhi_t1"), "outer": sem("hhi_outer")}
        hlo_ready = {"t1": sem("hlo_t1"), "outer": sem("hlo_outer")}
        inner = {1: sem("inner1"), 2: sem("inner2")}
        z_ready = {1: sem("z1_ready"), 2: sem("z2_ready")}
        res_ready = sem("res_ready")
        joined = {1: sem("joined1"), 2: sem("joined2")}
        outer = {1: sem("outer1"), 2: sem("outer2")}
        hidden_ready = sem("hidden_ready")
        out_ready = sem("out_ready")
        stored = [sem("stored_a"), sem("stored_b")]

        x_rows = x.rearrange("n c (j p) w -> n p c j w", p=2)
        out_rows = out.rearrange("n c (j p) w -> n p c j w", p=2)

        hid_data = hidden[:, 0:2 * (HPLANE + 1)].rearrange("p (s r) -> p s r", s=2)[:, :, 0:NP * (WQ + 1)] \
            .rearrange("p s (r c) -> p s r c", c=WQ + 1)
        hid_cols = hidden[:, 0:2 * HPLANE].rearrange("p (s r) -> p s r", s=2)[:, :, 0:NP * (WQ + 1)] \
            .rearrange("p s (r c) -> p s r c", c=WQ + 1)

        def wait(eng, semaphore, value):
            if isinstance(value, int) and value <= 0:
                return
            eng.wait_ge(semaphore, value)

        def run(eng, step):
            for s in (-1, 0, 1):
                step(s, s % 4)
            with eng.Fori(0, (N - 4) // 4) as turn:
                for k in range(4):
                    step(turn * 4 + (2 + k), (2 + k) % 4)
            for s in range(N - 2, N + 2):
                step(s, s % 4)

        def is_step(s, number):
            return isinstance(s, int) and s == number

        def there_is(s, image):
            return not isinstance(s, int) or 0 <= image < N

        X_BLOCKS = ((0, 0, 1, 0), (0, 1, 0, 0), (0, 1, 1, 1), (1, 0, 0, 1), (1, 0, 1, 2), (1, 1, 0, 2))
        HID_BLOCKS = ((0, 0, 0, 1), (0, 0, 1, 0), (0, 1, 0, 0), (1, 0, 1, 2), (1, 1, 0, 2), (1, 1, 1, 1))

        FILTERS = {"inner1": (1, slice(1, 3)), "outer1": (1, slice(0, 4, 3)), "all2": (2, slice(0, 4))}

        def chain(eng, semaphore):
            done = [0]

            def after(ins):
                done[0] += 1
                ins.then_inc(semaphore, 1)
                eng.wait_ge(semaphore, done[0])
            return after

        def double_inner_filters(eng, conv, after):
            w, g, total = w_raw[conv], g_t[conv], g_sum[conv]
            after(eng.tensor_tensor(total[:], w[:, :, 0, :], w[:, :, 2, :], ALU.add))
            eng.tensor_tensor(g[:, 1], total[:], w[:, :, 1, :], ALU.add)
            after(eng.tensor_tensor(g[:, 2], total[:], w[:, :, 1, :], ALU.subtract))

        def double_outer_filters(conv):
            nc.scalar.wait_ge(w_in[conv], 16)
            nc.scalar.activation(g_t[conv][:, 0], w_raw[conv][:, :, 0, :], ACT.Copy, scale=2.0)
            nc.scalar.activation(g_t[conv][:, 3], w_raw[conv][:, :, 2, :], ACT.Copy,
                                 scale=-2.0).then_inc(outer_taps[conv], 1)

        def fill_matrix(copy, which, blocks):
            conv, filters = FILTERS[which]
            for far, ki, mo, kh in blocks:
                half = slice(ki * C, ki * C + C)
                ins = copy(wmat[conv][half, filters, far, mo * C:mo * C + C], g_t[conv][half, filters, kh, :])
            ins.then_inc(mat_filled[which], 1)

        def scale_matrix(eng, which):
            conv, filters = FILTERS[which]
            eng.wait_ge(mat_filled[which], 1)
            eng.wait_ge(scale_ready[conv], 1)
            part = wmat[conv][:, filters].rearrange("p i f (s c) -> p i (f s) c", c=C)
            row = inv[:, 2 + (conv - 1) * C:2 + conv * C]
            scale = row.unsqueeze(1).unsqueeze(1).broadcast_to((P, part.shape[1], 4, C))
            eng.tensor_tensor(part, part, scale, ALU.mult).then_inc(mat_ready[which], 1)

        def high_weights(which):
            conv, part = FILTERS[which]
            nc.scalar.wait_ge(mat_ready[which], 1)
            nc.scalar.activation(w_hi[conv][:, part], wmat[conv][:, part], ACT.Copy).then_inc(whi_ready[which], 1)

        def low_weights(eng, which):
            conv, part = FILTERS[which]
            eng.wait_ge(whi_ready[which], 1)
            eng.tensor_tensor(w_lo[conv][:, part], wmat[conv][:, part], w_hi[conv][:, part].bitcast(F32),
                              ALU.subtract).then_inc(wlo_ready[which], 1)

        def newton_step(eng, after, part):
            after(eng.tensor_tensor(tmp[:, part], inv[:, part], inv[:, part], ALU.mult))
            after(eng.tensor_tensor(tmp[:, part], tmp[:, part], var[:, part], ALU.mult))
            after(eng.tensor_scalar(tmp[:, part], tmp[:, part], -0.5, 1.5, ALU.mult, ALU.add))
            after(eng.tensor_tensor(inv[:, part], inv[:, part], tmp[:, part], ALU.mult))

        def x_columns(k, parity):
            return x_sb[:, k % XBUFS, :, 1:W + 1].rearrange("p j (q s) -> p j q s", s=2)[:, :, :, parity]

        def x_full(which, k):
            full, places = (x_outer[:], slice(0, 2)) if which == "outer" else (x_inner[:, k], slice(2, 4))
            return full.rearrange("p s j q -> p s (j q)"), places

        def x_part(t, k, places):
            return t[:, k % 2, places, 1:NQ + 1, :].rearrange("p s j q -> p s (j q)")

        def hidden_rows(half):
            return slice(0, NP) if half is None else slice(*HALF1[half])

        def hidden_parts(which, b, half=None):
            rows = hidden_rows(half)
            if which == "t1":
                return t_inner[:, 0, rows], t1_hi[:, rows], t1_lo[:, rows]
            return t_outer[:, :, rows], h_hi[:, b, :, rows], h_lo[:, b, :, rows]

        def before_conv2(n):
            return (2, n - 1) if isinstance(n, int) and n == N - 1 else (1, n + 1)

        def load_parity(eng, n, k, parity):
            eng.dma_start(x_sb[parity * C:parity * C + C, k % XBUFS, :, 1:W + 1],
                          x_rows[n, parity]).then_inc(x_in[k % XBUFS], 16)

        block = ctx.enter_context(nc.Block())

        @block.sync
        def _(sp):
            def store(n, half):
                j0, j1 = HALF2[half]
                wait(sp, out_ready, 2 * n + half + 1)
                for parity in range(2):
                    sp.dma_start(out_rows[n, parity][:, j0:j1, :],
                                 out_sb[parity * C:parity * C + C, half]).then_inc(stored[half], 16)

            sp.dma_start(bn[:], params).then_inc(bn_in, 16)
            load_parity(sp, 0, 0, 0)
            sp.dma_start(w_raw[2][:], w2).then_inc(w_in[2], 16)

            def step(s, k):
                if not isinstance(s, int) or s + 2 < N:
                    wait(sp, tx_ready["outer"], s + 3 - XBUFS)
                    for parity in range(2):
                        load_parity(sp, s + 2, k + 2, parity)
                if there_is(s, s - 2):
                    store(s - 2, 0)
                    store(s - 2, 1)

            run(sp, step)
            for half in range(2):
                sp.wait_ge(stored[half], 32 * N)

        @block.gpsimd
        def _(pool):
            nc.gpsimd.memset(wmat[1][:], 0.0).then_inc(mat_zeroed, 1)
            nc.gpsimd.memset(x_sb[:, :, :, 0:1], 0.0).then_inc(x_zeroed, 1)
            nc.gpsimd.memset(x_sb[:, :, :, W + 1:W + 2], 0.0).then_inc(x_zeroed, 1)
            for t in (x_hi, x_lo):
                for b in range(2):
                    for row in (0, NQ + 1):
                        nc.gpsimd.memset(t[:, b, :, row, :].bitcast(F32), 0.0).then_inc(zeroed, 1)
            nc.gpsimd.memset(hidden[:], 0.0).then_inc(zeroed, 1)
            nc.gpsimd.memset(wmat[2][:], 0.0).then_inc(mat_zeroed, 1)

            after, row = chain(pool, bn_step[2]), slice(2 + C, 2 + 2 * C)
            pool.wait_ge(inv_ready, 2)
            newton_step(pool, after, row)
            after(pool.tensor_tensor(inv[:, row], inv[:, row], bn[:, 8 + C:8 + 2 * C], ALU.mult))
            pool.tensor_scalar(inv[:, row], inv[:, row], 0.5, None, ALU.mult).then_inc(scale_ready[2], 1)

            scale_matrix(pool, "inner1")
            scale_matrix(pool, "outer1")

            after = chain(pool, prep[2])
            pool.wait_ge(w_in[2], 16)
            double_inner_filters(pool, 2, after)
            scale_matrix(pool, "all2")
            low_weights(pool, "all2")

        @block.vector
        def _(dve):
            dve.wait_ge(w_in[1], 16)
            double_inner_filters(dve, 1, chain(dve, prep[1]))
            dve.wait_ge(mat_zeroed, 1)
            fill_matrix(nc.vector.tensor_copy, "inner1", X_BLOCKS)

            after, part, row = chain(dve, bn_step[1]), slice(0, 2 + C), slice(2, 2 + C)
            dve.wait_ge(std_ready, 1)
            nc.vector.reciprocal(inv[:, part], inv[:, part]).then_inc(inv_ready, 1)
            nc.vector.reciprocal(inv[:, 2 + C:], inv[:, 2 + C:]).then_inc(inv_ready, 1)
            dve.wait_ge(inv_ready, 1)
            newton_step(dve, after, part)
            nc.vector.tensor_tensor(inv[:, 0:2], inv[:, 0:2], bn[:, 0:2], ALU.mult)
            after(nc.vector.tensor_tensor(inv[:, row], inv[:, row], bn[:, 8:8 + C], ALU.mult))
            nc.vector.tensor_scalar(inv[:, row], inv[:, row], 0.5, None, ALU.mult).then_inc(scale_ready[1], 1)
            after(nc.vector.tensor_tensor(bias[:], bn[:, 6:8], inv[:, 0:2], ALU.mult))
            nc.vector.tensor_tensor(bias[:], bn[:, 4:6], bias[:], ALU.subtract).then_inc(bias_ready, 1)

            def sum_x(n, k):
                dve.wait_ge(x_in[k % XBUFS], (n - k % XBUFS) * (32 // XBUFS) + 32)
                wait(dve, res_ready, 2 * (n - TBUFS) + 2)
                nc.vector.tensor_tensor(x_inner[:, k, 0], x_columns(k, 0), x_columns(k, 1), ALU.add)

            def difference_x(n, k):
                nc.vector.tensor_tensor(x_inner[:, k, 1], x_columns(k, 1), x_columns(k, 0),
                                        ALU.subtract).then_inc(tx_ready["inner"], 1)

            def outer_x(n, k):
                wait(dve, xlo_ready["outer"], n)
                rows = x_sb[:, k % XBUFS]
                if is_step(n, 0):
                    dve.wait_ge(x_zeroed, 2)
                nc.vector.tensor_tensor(x_outer[:].rearrange("p s j q -> p j q s"),
                                        rows[:, :, 0:W].rearrange("p j (q s) -> p j q s", s=2),
                                        rows[:, :, 2:W + 2].rearrange("p j (q s) -> p j q s", s=2),
                                        ALU.subtract).then_inc(tx_ready["outer"], 1)

            def split_x(which, n, k):
                full, places = x_full(which, k)
                dve.wait_ge(xhi_ready[which], n + 1)
                nc.vector.tensor_tensor(x_part(x_lo, k, places), full,
                                        x_part(x_hi, k, places).bitcast(F32),
                                        ALU.subtract).then_inc(xlo_ready[which], 1)

            def join(conv, n, half, before):
                r0, r1 = (HALF1, HALF2)[conv - 1][half]
                width = (r1 - r0) * WQ
                dve.wait_ge(z_ready[conv], 2 * n + half + 1)
                dve.wait_ge(inner[conv], 2 * (2 * n + half) + 2)
                wait(dve, *((hidden_ready if before[0] == 1 else out_ready), 2 * before[1] + half + 1))
                t1 = psum[:, half, SUM_T1, 0:width].unsqueeze(1).broadcast_to((P, 2, width))
                nc.vector.tensor_tensor(psum[:, half, EVEN:ODD + 1, 0:width], t1, z[:, half, :, 0:width],
                                        ALU.add).then_inc(joined[conv], 1)

            def sum_hidden(n, half=None):
                rows = hidden_rows(half)
                dve.wait_ge(hidden_ready, 2 * n + (2 if half is None else half + 1))
                wait(dve, inner[2], 4 * n)
                nc.vector.tensor_tensor(t_inner[:, 0, rows], hid_data[:, 0, rows, 0:WQ], hid_data[:, 1, rows, 0:WQ],
                                        ALU.add).then_inc(th_ready["t1"], 1)

            def difference_hidden(n, half=None):
                rows = hidden_rows(half)
                nc.vector.tensor_tensor(t_inner[:, 1, rows], hid_data[:, 1, rows, 0:WQ], hid_data[:, 0, rows, 0:WQ],
                                        ALU.subtract).then_inc(th_ready["t2"], 1)

            def outer_hidden(n, half=None):
                rows = hidden_rows(half)
                wait(dve, hlo_ready["outer"], n)
                nc.vector.tensor_tensor(t_outer[:, :, rows], hid_cols[:, :, rows, 0:WQ],
                                        hid_cols[:, :, rows, 1:WQ + 1], ALU.subtract).then_inc(th_ready["outer"], 1)

            def split_hidden(which, n, b, half=None):
                full, hi, lo = hidden_parts(which, b, half)
                dve.wait_ge(hhi_ready[which], n + 1 + (half or 0))
                nc.vector.tensor_tensor(lo, full, hi.bitcast(F32), ALU.subtract).then_inc(hlo_ready[which], 1)

            def step(s, k):
                ahead, now, last = there_is(s, s + 1), there_is(s, s), there_is(s, s - 1)
                ka, kl = (k + 1) % 4, (k + 3) % 4
                if is_step(s, N):
                    sum_hidden(N - 1, 0)
                    difference_hidden(N - 1, 0)
                    outer_hidden(N - 1, 0)
                    sum_hidden(N - 1, 1)
                    join(2, N - 2, 1, before_conv2(N - 2))
                    split_hidden("t1", N - 1, kl % 2, 0)
                    split_hidden("outer", N - 1, kl % 2, 0)
                    outer_hidden(N - 1, 1)
                    difference_hidden(N - 1, 1)
                    split_hidden("t1", N - 1, kl % 2, 1)
                    join(2, N - 1, 0, before_conv2(N - 1))
                    split_hidden("outer", N - 1, kl % 2, 1)
                    return
                if there_is(s, s - 2):
                    join(2, s - 2, 1, before_conv2(s - 2))
                if last:
                    sum_hidden(s - 1)
                    difference_hidden(s - 1)
                    outer_hidden(s - 1)
                if now:
                    join(1, s, 0, (2, s - 2))
                if ahead:
                    sum_x(s + 1, ka)
                if last:
                    split_hidden("t1", s - 1, kl % 2)
                if ahead:
                    difference_x(s + 1, ka)
                if now:
                    join(1, s, 1, (2, s - 2))
                if ahead:
                    outer_x(s + 1, ka)
                if last:
                    split_hidden("outer", s - 1, kl % 2)
                if is_step(s, -1):
                    low_weights(dve, "inner1")
                if ahead:
                    split_x("inner", s + 1, ka)
                if last:
                    join(2, s - 1, 0, before_conv2(s - 1))
                if is_step(s, -1):
                    low_weights(dve, "outer1")
                if ahead:
                    split_x("outer", s + 1, ka)

            run(dve, step)

        @block.scalar
        def _(act):
            act.dma_start(w_raw[1][:], w1).then_inc(w_in[1], 16)
            load_parity(act, 0, 0, 1)
            act.wait_ge(bn_in, 16)
            nc.scalar.activation(var[:, 0:2], bn[:, 2:4], ACT.Copy, bias=EPS)
            nc.scalar.activation(var[:, 2:], bn[:, 8 + 2 * C:], ACT.Copy, bias=EPS).then_inc(var_ready, 1)
            act.wait_ge(var_ready, 1)
            nc.scalar.activation(inv[:], var[:], ACT.Sqrt).then_inc(std_ready, 1)

            def copy(to, taps):
                return nc.scalar.activation(to, taps, ACT.Copy)

            double_outer_filters(1)
            act.wait_ge(outer_taps[1], 1)
            act.wait_ge(mat_zeroed, 1)
            fill_matrix(copy, "outer1", X_BLOCKS)
            double_outer_filters(2)
            high_weights("inner1")

            def high_x(which, n, k):
                full, places = x_full(which, k)
                act.wait_ge(tx_ready[which], n + 1)
                wait(act, outer[1], 2 * (n - 1))
                nc.scalar.activation(x_part(x_hi, k, places), full, ACT.Copy).then_inc(xhi_ready[which], 1)

            def residual(n, k, half):
                j0, j1 = HALF2[half]
                width = (j1 - j0) * WQ
                before = before_conv2(n)
                act.wait_ge(joined[before[0]], 2 * before[1] + half + 1)
                for i, bank, share in ((0, SUM_T1, 0.5), (1, SUM_T2, -0.5)):
                    ins = nc.scalar.activation(psum[:, half, bank, 0:width],
                                               x_inner[:, k, i, j0:j1, :].rearrange("p j q -> p (j q)"),
                                               ACT.Copy, scale=share)
                ins.then_inc(res_ready, 1)

            def high_hidden(which, n, b, half=None):
                full, hi, _ = hidden_parts(which, b, half)
                act.wait_ge(th_ready[which], n + 1 + (half or 0))
                wait(act, *((inner[2], 4 * n) if which == "t1" else (outer[2], 2 * (n - 1))))
                nc.scalar.activation(hi, full, ACT.Copy).then_inc(hhi_ready[which], 1)

            def copy_sum(conv, n, half):
                r0, r1 = (HALF1, HALF2)[conv - 1][half]
                width = (r1 - r0) * WQ
                act.wait_ge(inner[conv], 2 * (2 * n + half) + 1)
                t2 = psum[:, half, SUM_T2, 0:width]
                nc.scalar.activation(z[:, half, 0, 0:width], t2, ACT.Identity, bias=bias[:, conv - 1:conv])
                nc.scalar.activation(z[:, half, 1, 0:width], t2, ACT.Identity, bias=bias[:, conv - 1:conv],
                                     scale=-1.0).then_inc(z_ready[conv], 1)

            def relu(rows, pairs, sums):
                return nc.scalar.activation(hid_data[rows, :, pairs, 0:WQ], sums[rows], ACT.Relu)

            def relu_hidden(n, half):
                k0, k1 = HALF1[half]
                act.wait_ge(outer[1], 2 * n + half + 1)
                wait(act, th_ready["outer"], n)
                src = psum[:, half, EVEN:ODD + 1, 0:(k1 - k0) * WQ].rearrange("p s (r q) -> p s r q", q=WQ)
                if half == 0:
                    relu(slice(0, C), 0, src[:, :, 0, :])
                    relu(slice(0, P), slice(1, k1), src[:, :, 1:, :]).then_inc(hidden_ready, 1)
                else:
                    end = k1 - k0 - 1
                    relu(slice(C, P), NP - 1, src[:, :, end, :])
                    relu(slice(0, P), slice(k0, NP - 1), src[:, :, 0:end, :]).then_inc(hidden_ready, 1)

            def relu_out(n, half):
                j0, j1 = HALF2[half]
                act.wait_ge(outer[2], 2 * n + half + 1)
                wait(act, stored[half], 32 * n)
                nc.scalar.activation(
                    out_sb[:, half].rearrange("p j (q s) -> p s j q", s=2),
                    psum[:, half, EVEN:ODD + 1, 0:(j1 - j0) * WQ].rearrange("p s (j q) -> p s j q", q=WQ),
                    ACT.Relu).then_inc(out_ready, 1)

            def step(s, k):
                ahead, now, last = there_is(s, s + 1), there_is(s, s), there_is(s, s - 1)
                ka, kl = (k + 1) % 4, (k + 3) % 4
                if is_step(s, N):
                    residual(N - 1, kl, 0)
                    high_hidden("t1", N - 1, kl % 2, 0)
                    relu_hidden(N - 1, 1)
                    high_hidden("outer", N - 1, kl % 2, 0)
                    relu_out(N - 2, 0)
                    copy_sum(2, N - 1, 0)
                    high_hidden("t1", N - 1, kl % 2, 1)
                    residual(N - 1, kl, 1)
                    high_hidden("outer", N - 1, kl % 2, 1)
                    relu_out(N - 2, 1)
                    copy_sum(2, N - 1, 1)
                    return
                if is_step(s, 0):
                    act.wait_ge(prep[2], 2)
                    act.wait_ge(outer_taps[2], 1)
                    act.wait_ge(mat_zeroed, 2)
                    fill_matrix(copy, "all2", HID_BLOCKS)
                    act.wait_ge(bias_ready, 1)
                    act.wait_ge(zeroed, 9)
                if last:
                    relu_hidden(s - 1, 1)
                if now:
                    copy_sum(1, s, 0)
                if last:
                    high_hidden("t1", s - 1, kl % 2)
                if there_is(s, s - 2):
                    relu_out(s - 2, 0)
                if now:
                    copy_sum(1, s, 1)
                if last:
                    residual(s - 1, kl, 0)
                if there_is(s, s - 2):
                    relu_out(s - 2, 1)
                if last:
                    high_hidden("outer", s - 1, kl % 2)
                    copy_sum(2, s - 1, 0)
                    residual(s - 1, kl, 1)
                if is_step(s, 0):
                    high_weights("all2")
                if ahead:
                    high_x("inner", s + 1, ka)
                if is_step(s, -1):
                    high_weights("outer1")
                if now:
                    relu_hidden(s, 0)
                if ahead:
                    high_x("outer", s + 1, ka)
                if last:
                    copy_sum(2, s - 1, 1)

            run(act, step)

        @block.tensor
        def _(pe):
            def sum_products(conv, half, i, bank, passes, onto):
                r0, r1 = (HALF1, HALF2)[conv - 1][half]
                width = (r1 - r0) * WQ
                todo = [(far, t, w) for far in range(2) for t, w in passes]
                for at, (far, t, w) in enumerate(todo):
                    moving = t[:, r0 + far:r1 + far, :].rearrange("p r q -> p (r q)")
                    ins = nc.tensor.matmul(psum[:, half, bank, 0:width], w[:, i, far, :], moving,
                                           start=not onto and at == 0, stop=at == len(todo) - 1,
                                           skip_group_check=onto)
                return ins

            def passes_of(conv, i, b):
                if (conv, i) == (2, 2):
                    return ((t_inner[:, 1], wmat[2]),)
                if conv == 1:
                    place = (OUTER[1] | {1: 2, 2: 3})[i]
                    hi, lo = x_hi[:, b, place], x_lo[:, b, place]
                elif i == 1:
                    hi, lo = t1_hi, t1_lo
                else:
                    hi, lo = h_hi[:, b, OUTER[2][i]], h_lo[:, b, OUTER[2][i]]
                return (hi, w_hi[conv]), (hi, w_lo[conv]), (lo, w_hi[conv])

            def inner_products_2(n, half, more=0):
                pe.wait_ge(th_ready["t2"], n + 1 + more)
                pe.wait_ge(res_ready, 2 * n + half + 1)
                sum_products(2, half, 2, SUM_T2, passes_of(2, 2, 0), True).then_inc(inner[2], 1)
                pe.wait_ge(hlo_ready["t1"], n + 1 + more)
                sum_products(2, half, 1, SUM_T1, passes_of(2, 1, 0), True).then_inc(inner[2], 1)

            def outer_products(conv, n, b, half):
                pe.wait_ge(joined[conv], 2 * n + half + 1)
                for i, bank in ((0, EVEN), (3, ODD)):
                    ins = sum_products(conv, half, i, bank, passes_of(conv, i, b), True)
                ins.then_inc(outer[conv], 1)

            pe.wait_ge(zeroed, 9)
            for half in range(2):
                for bank in (EVEN, ODD):
                    nc.tensor.matmul(psum[:, half, bank, 0:MAXN], hidden[:, 0:P], hidden[:, 0:MAXN],
                                     start=True, stop=True).then_inc(bits_set, 1)
            for _ in range(WARM_UP):
                nc.tensor.matmul(psum[:, 1, ODD, 0:MAXN], hidden[:, 0:P], hidden[:, 0:MAXN],
                                 start=True, stop=True).then_inc(bits_set, 1)
            pe.wait_ge(wlo_ready["inner1"], 1)

            def step(s, k):
                now, last, store = there_is(s, s), there_is(s, s - 1), there_is(s, s - 2)
                if is_step(s, N):
                    for half in range(2):
                        outer_products(2, N - 2, k % 2, half)
                        inner_products_2(N - 1, half, half)
                    return
                for half in range(2):
                    if now:
                        pe.wait_ge(xlo_ready["inner"], s + 1)
                        wait(pe, joined[2], 2 * (s - 2) + half + 1)
                        for i, bank in ((2, SUM_T2), (1, SUM_T1)):
                            sum_products(1, half, i, bank, passes_of(1, i, k % 2), False).then_inc(inner[1], 1)
                    if store:
                        pe.wait_ge(hlo_ready["outer"], s if is_step(s, N + 1) else s - 1)
                        outer_products(2, s - 2, k % 2, half)
                if is_step(s, 1):
                    pe.wait_ge(wlo_ready["all2"], 1)
                for half in range(2):
                    if last:
                        inner_products_2(s - 1, half)
                    if is_step(s, 0):
                        pe.wait_ge(wlo_ready["outer1"], 1)
                    if now:
                        pe.wait_ge(xlo_ready["outer"], s + 1)
                        outer_products(1, s, k % 2, half)

            run(pe, step)


def kernel(**inputs):
    import numpy as np
    import concourse.bacc as bacc
    from concourse.bass_utils import run_bass_kernel_spmd

    given = {name: np.asarray(a) for name, a in inputs.items()}
    arrays = {"x": np.ascontiguousarray(given["x"])}
    for layer in (1, 2):
        w = np.transpose(given[f"L0_conv_w{layer}"], (1, 2, 3, 0))
        arrays[f"w{layer}"] = np.ascontiguousarray(np.concatenate([w, w]))
    columns = np.stack([given[f"L0_conv_{name}{layer}"] for name in "gvbm" for layer in (1, 2)], axis=1)
    columns = np.concatenate([columns, columns])
    row = np.concatenate([given[f"L0_conv_{name}{layer}"] for name in "gv" for layer in (1, 2)])
    arrays["params"] = np.concatenate([columns, np.broadcast_to(row, (len(columns), len(row)))], axis=1)

    nc = bacc.Bacc("TRN2", target_bir_lowering=False, num_devices=1)
    dram = {name: nc.dram_tensor(f"{name}_dram", a.shape, mybir.dt.from_np(a.dtype), kind="ExternalInput").ap()
             for name, a in arrays.items()}
    out = nc.dram_tensor("out_dram", arrays["x"].shape, F32, kind="ExternalOutput").ap()
    residual_block(nc, dram["x"], dram["w1"], dram["w2"], dram["params"], out)
    result = run_bass_kernel_spmd(nc, [{f"{name}_dram": a for name, a in arrays.items()}], core_ids=[0])
    return result.results[0]["out_dram"]
```
